# Optimizing a Trainium2 kernel written in Bass

```python
import numpy as np
import jax
import jax.numpy as jnp

def _softmax(x, axis=-1):
    return jax.nn.softmax(x, axis=axis)

def _gelu(x):
    return jax.nn.gelu(x, approximate=True)

def _silu(x):
    return jax.nn.silu(x)

def _sigmoid(x):
    return jax.nn.sigmoid(x)

def _layernorm(x, axis=-1, eps=1e-05):
    m = jnp.mean(x, axis=axis, keepdims=True)
    v = jnp.var(x, axis=axis, keepdims=True)
    return (x - m) / jnp.sqrt(v + eps)

def _scatter_add(tgt, idx, src, axis=0):
    return tgt.at[idx].add(src)

def _segment_sum(src, seg, n):
    return jax.ops.segment_sum(src, seg, n)
kernel_name = 'mk_adj_ffn_d1_adj_r2_043386'

def setup_inputs(seed: int=0):
    np.random.seed(seed)
    _w = jnp.asarray

    def _rec_inputs():
        import jax
        import jax.numpy as jnp
        _gk = jax.random.key(seed)
        x = -0.0002928 + 1 * jax.random.normal(jax.random.fold_in(_gk, 1), (64, 128, 128), jnp.float32)
        _w = (1.0 + jnp.arange(128, dtype=jnp.float32)) ** (-0.5)
        _w = _w / _w.mean()
        _pij = jnp.clip(0.125 * _w[:, None] * _w[None, :], 0.0, 1.0)
        _a = jax.random.uniform(jax.random.fold_in(_gk, 2), (64, 128, 128)) < _pij
        adj = _a.astype(jnp.int32)
        return (x, adj)
    x, adj = _rec_inputs()

    def _L0_gnn_setup():
        import jax, jax.numpy as jnp
        import numpy as np
        B, N, D_IN, D_OUT, R = (8, 1024, 128, 128, 4)
        key = jax.random.key(seed)
        k1, k2, k3, k4 = jax.random.split(key, 4)
        x = jax.random.normal(k1, (B, N, D_IN), dtype=jnp.float32)
        adj = jnp.zeros((1,), dtype=jnp.float32)
        relation = jax.random.randint(k2, (B, N, N), 0, R + 1, dtype=jnp.int32)
        weight = jax.random.normal(k3, (R, D_IN, D_OUT), dtype=jnp.float32) * 0.05
        bias = jax.random.normal(k4, (D_OUT,), dtype=jnp.float32) * 0.05
        return {'x': x, 'adj': adj, 'relation': relation, 'weight': weight, 'bias': bias}
    _L0_gnn_all = _L0_gnn_setup()
    _L0_gnn_in = {k: v for k, v in _L0_gnn_all.items() if k in ('adj', 'weight', 'bias')}
    del _L0_gnn_all

    def _L0_ffn_setup():
        import jax, jax.numpy as jnp
        import numpy as np
        C = 128
        EPS = 1e-05
        N_ITERS = 30

        def _layernorm(x, w, bias):
            mu = jnp.mean(x, axis=-1, keepdims=True)
            var = jnp.mean(jnp.square(x - mu), axis=-1, keepdims=True)
            return (x - mu) * jax.lax.rsqrt(var + EPS) * w + bias
        key = jax.random.key(seed)
        kx, kw, kb, klw, klb = jax.random.split(key, 5)
        x = jax.random.normal(kx, (8, 1024, C), dtype=jnp.float32)
        bound = 1.0 / np.sqrt(C)
        W = jax.random.uniform(kw, (C, C), minval=-bound, maxval=bound, dtype=jnp.float32)
        b = jax.random.uniform(kb, (C,), minval=-bound, maxval=bound, dtype=jnp.float32)
        ln_w = jnp.ones((C,), dtype=jnp.float32)
        ln_b = jnp.zeros((C,), dtype=jnp.float32)
        return {'x': x, 'ln_w': ln_w, 'ln_b': ln_b, 'W': W, 'b': b}
    _L0_ffn_all = _L0_ffn_setup()
    _L0_ffn_in = {k: v for k, v in _L0_ffn_all.items() if k in ('ln_w', 'ln_b', 'W', 'b')}
    del _L0_ffn_all
    return {'x': x, 'adj': adj, 'L0_gnn_adj': _L0_gnn_in['adj'], 'L0_gnn_weight': _L0_gnn_in['weight'], 'L0_gnn_bias': _L0_gnn_in['bias'], 'L0_ffn_ln_w': _L0_ffn_in['ln_w'], 'L0_ffn_ln_b': _L0_ffn_in['ln_b'], 'L0_ffn_W': _L0_ffn_in['W'], 'L0_ffn_b': _L0_ffn_in['b']}

def reference(x, adj, L0_gnn_adj, L0_gnn_weight, L0_gnn_bias, L0_ffn_ln_w, L0_ffn_ln_b, L0_ffn_W, L0_ffn_b):
    import jax
    import jax.numpy as jnp

    def _L0_gnn_ref(x, adj, relation, weight, bias):
        import jax, jax.numpy as jnp
        import numpy as np
        B, N, D_IN, D_OUT, R = (8, 1024, 128, 128, 4)
        rel_ids = jnp.arange(1, weight.shape[0] + 1, dtype=relation.dtype)
        masks = (relation[None] == rel_ids[:, None, None, None]).astype(x.dtype)
        h = jnp.einsum('rbnm,bmd->rbnd', masks, x)
        y = jnp.einsum('rbnd,rdo->bno', h, weight)
        return y + bias

    def _L0_ffn_ref(x, ln_w, ln_b, W, b):
        import jax, jax.numpy as jnp
        import numpy as np
        C = 128
        EPS = 1e-05
        N_ITERS = 30

        def _layernorm(x, w, bias):
            mu = jnp.mean(x, axis=-1, keepdims=True)
            var = jnp.mean(jnp.square(x - mu), axis=-1, keepdims=True)
            return (x - mu) * jax.lax.rsqrt(var + EPS) * w + bias

        def step(h, _):
            h = h + 0.01 * jnp.tanh(h)
            h = h * jax.nn.sigmoid(h)
            h = _layernorm(h, ln_w, ln_b)
            h = jnp.einsum('bsc,dc->bsd', h, W) + b
            return (h, None)
        x, _ = jax.lax.scan(step, x, None, length=N_ITERS)
        return x
    x = x + _L0_gnn_ref(_layernorm(x, axis=-1), L0_gnn_adj, adj, L0_gnn_weight, L0_gnn_bias)
    x = x + _L0_ffn_ref(_layernorm(x, axis=-1), L0_ffn_ln_w, L0_ffn_ln_b, L0_ffn_W, L0_ffn_b)
    return x

_drawn_inputs = setup_inputs


def setup_inputs(seed=0):
    import zlib

    import numpy as np

    out = dict(_drawn_inputs(seed))
    spreads = {'L0_ffn_ln_w': (1.0, 0.2), 'L0_ffn_ln_b': (0.0, 0.1)}
    factors = {}
    for name, (base, spread) in spreads.items():
        noise = np.random.default_rng([zlib.crc32(name.encode()), seed]).standard_normal(out[name].shape)
        drawn = base * np.exp(spread * noise) if base else spread * noise
        out[name] = jnp.asarray(drawn.astype(out[name].dtype))
    for name, factor in factors.items():
        out[name] = (out[name] * factor).astype(out[name].dtype)
    return out
```

```python
import math
from contextlib import ExitStack

import numpy as np
import concourse.bass as bass
from concourse import mybir

FP32 = mybir.dt.float32
BF16 = mybir.dt.bfloat16
I32 = mybir.dt.int32
ALU = mybir.AluOpType
ACT = mybir.ActivationFunctionType
AX = mybir.AxisListType

P = 128
B = 64
R = 4
STEPS = 30
EPS = 1e-5
BANK = 512

GROUP = BANK // P
TG = 8
TILE = TG * P
TILES = B // TG
PAIR = 2 * TG
GROUPS = PAIR // GROUP
PAIRS = B // PAIR

ROOT = math.sqrt(P)
MAGIC = 1597463007.0
NEWTON = 3
CHAIN = 5 + 3 * NEWTON
HSCALE = 100.0
TAU = 0.01

LAG_Z, LAG_MM, LAG_EV = 3, 4, 7


def at(it, n):
    return isinstance(it, int) and it == n


def build(nc, x, adj, gw, gb, ln_w, ln_b, fw, fb, out):
    ctx = ExitStack()
    with ctx:
        def sb(name, shape, dt=FP32):
            return ctx.enter_context(nc.sbuf_tensor(name, shape, dt))

        def sem(name):
            return ctx.enter_context(nc.semaphore(name))

        x_v = x.rearrange("b n c -> n b c")
        adj_v = adj.rearrange("b n m -> n b m")
        out_v = out.rearrange("b n c -> n b c")

        ident = sb("ident", [P, P])
        ident_b = sb("ident_b", [P, P], BF16)
        gw_sb = sb("gw_sb", [P, R, P])
        gb_sb = sb("gb_sb", [P, 1])
        fw_sb = sb("fw_sb", [P, P])
        fb_sb = sb("fb_sb", [P, 1])
        lnw_row = sb("lnw_row", [P, P])
        lnb_row = sb("lnb_row", [P, P])
        fww = sb("fww", [P, P])
        fwb = sb("fwb", [P, P])
        wsum = sb("wsum", [P, 1])
        bsum = sb("bsum", [P, 1])
        wcent = sb("wcent", [P, P])
        weff = sb("weff", [P, P])
        cent = sb("cent", [P, P])
        bias100 = sb("bias100", [P, 1])
        zero = sb("zero", [P, 1])

        x_in = sb("x_in", [P, 2, TG, P])
        adj_in = sb("adj_in", [P, 2, TG, P], I32)
        adj_b = sb("adj_b", [P, GROUPS, BANK], BF16)
        adj_t = sb("adj_t", [P, GROUPS, BANK], BF16)
        mask = sb("mask", [P, GROUPS, R, BANK], BF16)
        xn = sb("xn", [P, GROUPS, BANK])
        xres = sb("xres", [P, GROUPS, BANK])
        part = sb("part", [P, GROUPS, 3, BANK], BF16)
        h_sb = sb("h_sb", [P, 2, R, GROUP, P])
        rstd = sb("rstd", [P, PAIR])
        nmr = sb("nmr", [P, PAIR])
        msum = sb("msum", [P, PAIR])

        x1_flat = sb("x1", [P, B * P])
        x1 = x1_flat[:].rearrange("p (k t) -> p k t", k=TILES)
        H = sb("H", [P, TILES, TILE])
        T = sb("T", [P, 2, TILE])
        U = sb("U", [P, 2, TILE])
        g = H
        z = sb("z", [P, 2, TILE])
        fin = sb("fin", [P, 2, TILE])
        o_sb = sb("o_sb", [P, 2, TILE])
        st = sb("st", [P, 2, PAIR, 6])
        nv = sb("nv", [P, PAIR])
        nd = sb("nd", [P, PAIR])
        nt = sb("nt", [P, PAIR])
        ny = sb("ny", [P, 2, PAIR])

        ps = ctx.enter_context(nc.psum_tensor("ps", [P, 8, BANK], FP32))
        adj_ps = [ps[:, b, 0:BANK // 2].bitcast(BF16) for b in (0, 1)]
        h_ps = [ps[:, 2 + j, :] for j in range(GROUP)]
        xt_ps = ps[:, 6, :]
        y_ps = ps[:, 7, :]
        gt_ps = [ps[:, 0:2, :].rearrange("p a b -> p (a b)"), ps[:, 2:4, :].rearrange("p a b -> p (a b)")]
        rb_ps = ps[:, 4:6, :].rearrange("p a b -> p (a b)")
        mm_ps = ps[:, 6:8, :].rearrange("p a b -> p (a b)")

        s_w = sem("s_w")
        s_x = [sem("s_xin0"), sem("s_xin1")]
        s_adj = [sem("s_adj0"), sem("s_adj1")]
        s_id0 = sem("s_id0")
        s_id = sem("s_id")
        s_prep = sem("s_prep")
        s_wc = sem("s_wc")
        s_wt = sem("s_wt")
        s_we = sem("s_we")
        s_xbn = sem("s_xbn")
        s_chain = sem("s_chain")
        s_m = sem("s_m")
        s_ln = sem("s_ln")
        s_cast = sem("s_cast")
        s_xs = sem("s_xs")
        s_xn = sem("s_xn")
        s_hi = sem("s_hi")
        s_res = sem("s_res")
        s_mid = sem("s_mid")
        s_lo = sem("s_lo")
        s_at = sem("s_at")
        s_ate = sem("s_ate")
        s_xt = sem("s_xt")
        s_xte = sem("s_xte")
        s_mask = sem("s_mask")
        s_h = sem("s_h")
        s_hea = sem("s_hea")
        s_hed = sem("s_hed")
        s_y = sem("s_y")
        s_x1 = sem("s_x1")
        s_tanh = sem("s_tanh")
        s_add = sem("s_add")
        s_silu = sem("s_silu")
        s_tr = sem("s_tr")
        s_bn = sem("s_bn")
        s_bc = sem("s_bc")
        s_z = sem("s_z")
        s_mm = sem("s_mm")
        s_ev = sem("s_ev")
        s_fin = sem("s_fin")
        s_ot = sem("s_ot")
        s_oe = sem("s_oe")
        s_out = [sem("s_out0"), sem("s_out1")]

        block = ctx.enter_context(nc.Block())
        N_W = 6
        EV_D = GROUP - 1

        @block.sync
        def _(sp):
            def load_pair(it, first):
                for t in range(2):
                    if not first:
                        sp.wait_ge(s_xn, it * GROUPS + 2 * t + 2 - GROUPS)
                        sp.wait_ge(s_xt, it * GROUPS + 2 * t + 2 - GROUPS)
                    sp.dma_start(x_in[:, t], x_v[:, bass.ds(it * PAIR + t * TG, TG), :]).then_inc(s_x[t], 16)
                    if not first:
                        sp.wait_ge(s_cast, it * GROUPS + 2 * t + 2 - GROUPS)
                    sp.dma_start(adj_in[:, t], adj_v[:, bass.ds(it * PAIR + t * TG, TG), :]).then_inc(s_adj[t], 16)

            load_pair(0, True)
            sp.dma_start(gw_sb[:], gw.rearrange("r d o -> d r o")).then_inc(s_w, 16)
            sp.dma_start(gb_sb[:], gb.rearrange("(o a) -> o a", a=1)).then_inc(s_w, 16)
            sp.dma_start(fw_sb[:], fw).then_inc(s_w, 16)
            sp.dma_start(fb_sb[:], fb.rearrange("(o a) -> o a", a=1)).then_inc(s_w, 16)
            sp.dma_start(lnw_row[:], ln_w.rearrange("(a c) -> a c", a=1).to_broadcast([P, P])).then_inc(s_w, 16)
            sp.dma_start(lnb_row[:], ln_b.rearrange("(a c) -> a c", a=1).to_broadcast([P, P])).then_inc(s_w, 16)
            with sp.Fori(1, PAIRS) as it:
                load_pair(it, False)
            for k in range(TILES):
                sp.wait_ge(s_oe, k + 1)
                sp.dma_start(out_v[:, k * TG:(k + 1) * TG, :],
                             o_sb[:, k % 2].rearrange("p (b c) -> p b c", c=P)).then_inc(s_out[k % 2], 16)
            for a in range(2):
                sp.wait_ge(s_out[a], 16 * TILES // 2)

        @block.gpsimd
        def _(pool):
            nc.gpsimd.memset(ident[:], 0.0)
            nc.gpsimd.memset(ident_b[:], 0.0).then_inc(s_id0, 1)
            pool.wait_ge(s_id0, 1)
            for m in (ident, ident_b):
                last = nc.gpsimd.affine_select(out=m[:], in_=m[:], compare_op=ALU.not_equal, fill=1.0,
                                               base=0, pattern=[[-1, P]], channel_multiplier=1)
            last.then_inc(s_id, 1)

            def prepare(it, first):
                for q in range(GROUPS):
                    t, o = q // 2, (q % 2) * GROUP
                    n = it * GROUPS + q
                    b = slice(q * GROUP, (q + 1) * GROUP)
                    dst = xn[:, q].rearrange("p (b c) -> p b c", c=P)
                    if q == 0:
                        pool.wait_ge(s_ln, it + 1)
                    if not first:
                        pool.wait_ge(s_res, n + 1 - GROUPS)
                    nc.gpsimd.tensor_tensor(dst, x_in[:, t, o:o + GROUP, :],
                                            rstd[:, b].unsqueeze(2).to_broadcast([P, GROUP, P]),
                                            ALU.mult).then_inc(s_xs, 1)
                    pool.wait_ge(s_xs, n + 1)
                    nc.gpsimd.tensor_tensor(dst, dst, nmr[:, b].unsqueeze(2).to_broadcast([P, GROUP, P]),
                                            ALU.add).then_inc(s_xn, 1)

            prepare(0, True)
            with pool.Fori(1, PAIRS) as it:
                prepare(it, False)

            def add(it, k, early):
                pool.wait_ge(s_tanh, (it - 1) * TILES + k + 1)
                if not (early and k < 2):
                    pool.wait_ge(s_silu, (it - 1) * TILES + k - 1)
                nc.gpsimd.tensor_tensor(U[:, k % 2], H[:, k], T[:, k % 2], ALU.add).then_inc(s_add, 1)

            for k in range(TILES):
                add(1, k, True)
            with pool.Fori(2, STEPS + 1) as it:
                for k in range(TILES):
                    add(it, k, False)

        @block.scalar
        def _(act):
            act.wait_ge(s_w, 16 * N_W)

            def cast(n, q, it, first):
                act.wait_ge(s_adj[q // 2], it * 16 + 16)
                if not first:
                    act.wait_ge(s_at, n + 1 - GROUPS)
                o = (q % 2) * GROUP
                nc.scalar.copy(adj_b[:, q].rearrange("p (b m) -> p b m", m=P),
                               adj_in[:, q // 2, o:o + GROUP, :]).then_inc(s_cast, 1)

            def prepare_a(n, q, it, first):
                act.wait_ge(s_at, n + 1)
                if not first:
                    act.wait_ge(s_mask, n + 1 - GROUPS)
                nc.scalar.copy(adj_t[:, q], adj_ps[q % 2]).then_inc(s_ate, 1)
                act.wait_ge(s_xt, n + 1)
                nc.scalar.activation(x1_flat[:, bass.ds(n * BANK, BANK)], xt_ps, ACT.Identity,
                                     bias=gb_sb[:, 0:1]).then_inc(s_xte, 1)

            def prepare_b(n, q, it, first):
                act.wait_ge(s_xn, n + 1)
                if not first:
                    act.wait_ge(s_h, (n + 1 - GROUPS) * GROUP)
                nc.scalar.copy(part[:, q, 0], xn[:, q]).then_inc(s_hi, 1)
                act.wait_ge(s_res, n + 1)
                nc.scalar.copy(part[:, q, 1], xres[:, q]).then_inc(s_mid, 1)

            def evacuate(m, q, early):
                if not early:
                    act.wait_ge(s_y, m - 1)
                for j in range(EV_D):
                    act.wait_ge(s_h, m * GROUP + j + 1)
                    nc.scalar.copy(h_sb[:, q % 2, :, j, :],
                                   h_ps[j].rearrange("p (r n) -> p r n", r=R)).then_inc(s_hea, 1)

            def both(it, early):
                cast(it * GROUPS, 0, it, False)
                for q in range(GROUPS):
                    n = it * GROUPS + q
                    if q + 1 < GROUPS:
                        cast(n + 1, q + 1, it, False)
                    prepare_a(n, q, it, False)
                    evacuate(n - GROUPS, q, early and q < 2)
                    prepare_b(n, q, it, False)

            for q in range(GROUPS):
                cast(q, q, 0, True)
            for q in range(GROUPS):
                prepare_a(q, q, 0, True)
                prepare_b(q, q, 0, True)
            act.wait_ge(s_wt, 1)
            nc.scalar.copy(weff[:], y_ps[:, 0:P]).then_inc(s_we, 1)
            both(1, True)
            with act.Fori(2, PAIRS) as it:
                both(it, False)
            for q in range(GROUPS):
                evacuate((PAIRS - 1) * GROUPS + q, q, False)

            def tanh(it, k, early):
                act.wait_ge(s_ev, it * TILES + k + 1 - TILES)
                if not early:
                    act.wait_ge(s_add, (it - 1) * TILES + k - 1)
                nc.scalar.activation(T[:, k % 2], H[:, k], ACT.Tanh, scale=1.0 / HSCALE).then_inc(s_tanh, 1)

            def silu(it, k):
                act.wait_ge(s_add, (it - 1) * TILES + k + 1)
                nc.scalar.activation(g[:, k], U[:, k % 2], ACT.Silu, scale=1.0 / HSCALE).then_inc(s_silu, 1)

            def evac(it, k):
                act.wait_ge(s_mm, it * TILES + k + 1)
                bias = zero if at(it, 0) else bias100
                nc.scalar.activation(H[:, k], mm_ps, ACT.Identity, bias=bias[:, 0:1],
                                     scale=HSCALE).then_inc(s_ev, 1)

            def slot(it, k, prev):
                if not at(it, 0) and not at(it, STEPS + 1):
                    tanh(it, k, at(it, 1) and k < 2)
                e = (k - LAG_EV) % TILES
                if k >= LAG_EV:
                    evac(it, e)
                elif prev is not None:
                    evac(prev, e)
                if k >= 1:
                    if not at(it, 0) and not at(it, STEPS + 1):
                        silu(it, k - 1)
                elif prev is not None and not at(prev, 0):
                    silu(prev, TILES - 1)

            act.wait_ge(s_wc, 1)
            for k in range(TILES):
                slot(0, k, None)
            for k in range(TILES):
                slot(1, k, 0)
            with act.Fori(2, STEPS + 1) as it:
                for k in range(TILES):
                    slot(it, k, it - 1)
            for k in range(LAG_EV):
                slot(STEPS + 1, k, STEPS)
            for k in range(TILES):
                act.wait_ge(s_ot, k + 1)
                if k >= 2:
                    act.wait_ge(s_out[k % 2], 16 * (k // 2))
                nc.scalar.copy(o_sb[:, k % 2], gt_ps[k % 2]).then_inc(s_oe, 1)

        @block.vector
        def _(dve):
            def step(ins, semaphore, value):
                ins.then_inc(semaphore, 1)
                dve.wait_ge(semaphore, value)

            nc.vector.memset(zero[:], 0.0)
            dve.wait_ge(s_w, 16 * N_W)
            dve.wait_ge(s_id, 1)
            nc.vector.tensor_tensor(fww[:], fw_sb[:], lnw_row[:], ALU.mult)
            step(nc.vector.tensor_tensor(fwb[:], fw_sb[:], lnb_row[:], ALU.mult), s_prep, 1)
            nc.vector.reduce_sum(wsum[:], fww[:], AX.X)
            step(nc.vector.reduce_sum(bsum[:], fwb[:], AX.X), s_prep, 2)
            step(nc.vector.tensor_scalar(wsum[:], wsum[:], 1.0 / P, None, ALU.mult), s_prep, 3)
            nc.vector.tensor_scalar(wcent[:], fww[:], wsum[:, 0:1], ROOT, ALU.subtract, ALU.mult)
            nc.vector.tensor_scalar(cent[:], ident[:], 1.0 / P, ROOT, ALU.subtract, ALU.mult)
            nc.vector.tensor_scalar(bias100[:], bsum[:], fb_sb[:, 0:1], HSCALE, ALU.add,
                                    ALU.mult).then_inc(s_wc, 1)

            def root(y, base):
                def link(ins, n):
                    step(ins, s_chain, base + n)

                def of(col):
                    return s_ap[:, :, col]
                s_ap = y[1]
                link(nc.vector.tensor_tensor(nd[:], of(1), of(4), ALU.subtract), 1)
                link(nc.vector.scalar_tensor_tensor(out=nt[:], in0=nd[:], scalar=P / 4.0, in1=nd[:],
                                                    op0=ALU.mult, op1=ALU.mult), 2)
                link(nc.vector.scalar_tensor_tensor(out=nd[:], in0=nt[:], scalar=P * EPS, in1=of(2),
                                                    op0=ALU.add, op1=ALU.add), 3)
                link(nc.vector.tensor_tensor(nv[:], nd[:], of(5), ALU.add), 4)
                link(nc.vector.tensor_scalar(y[0].bitcast(I32), nv[:].bitcast(I32), -0.5, MAGIC,
                                             ALU.mult, ALU.add), 5)
                for i in range(NEWTON):
                    link(nc.vector.tensor_tensor(nt[:], y[0], y[0], ALU.mult), 6 + 3 * i)
                    link(nc.vector.scalar_tensor_tensor(out=nd[:], in0=nt[:], scalar=-0.5, in1=nv[:],
                                                        op0=ALU.mult, op1=ALU.mult), 7 + 3 * i)
                    link(nc.vector.scalar_tensor_tensor(out=y[0], in0=nd[:], scalar=1.5, in1=y[0],
                                                        op0=ALU.add, op1=ALU.mult), 8 + 3 * i)

            def statistics(it, first):
                for b in range(PAIR):
                    if b % TG == 0:
                        dve.wait_ge(s_x[b // TG], it * 16 + 16)
                    last = nc.vector.bn_stats(st[:, 0, b], x_in[:, b // TG, b % TG])
                last.then_inc(s_xbn, 1)
                dve.wait_ge(s_xbn, it + 1)
                root((ny[:, 0], st[:, 0]), it * CHAIN)
                step(nc.vector.tensor_tensor(msum[:], st[:, 0, :, 1], st[:, 0, :, 4], ALU.add), s_m, it * 2 + 1)
                if not first:
                    dve.wait_ge(s_xn, it * GROUPS)
                step(nc.vector.tensor_scalar(rstd[:], ny[:, 0], ROOT, None, ALU.mult), s_m, it * 2 + 2)
                nc.vector.scalar_tensor_tensor(out=nmr[:], in0=msum[:], scalar=-0.5, in1=rstd[:],
                                               op0=ALU.mult, op1=ALU.mult).then_inc(s_ln, 1)

            def residual(n, q, first):
                dve.wait_ge(s_hi, n + 1)
                if not first:
                    dve.wait_ge(s_mid, n + 1 - GROUPS)
                nc.vector.tensor_tensor(xres[:, q], xn[:, q], part[:, q, 0], ALU.subtract).then_inc(s_res, 1)

            def low(n, q):
                dve.wait_ge(s_mid, n + 1)
                nc.vector.tensor_tensor(part[:, q, 2], xres[:, q], part[:, q, 1], ALU.subtract).then_inc(s_lo, 1)

            def masks(n, q, first):
                dve.wait_ge(s_ate, n + 1)
                if not first:
                    dve.wait_ge(s_h, (n + 1 - GROUPS) * GROUP)
                for r in range(R):
                    last = nc.vector.tensor_scalar(mask[:, q, r], adj_t[:, q], float(r + 1), None, ALU.is_equal)
                last.then_inc(s_mask, 1)

            def evacuate(m, q, early):
                if not early:
                    dve.wait_ge(s_y, m - 1)
                dve.wait_ge(s_h, (m + 1) * GROUP)
                nc.vector.tensor_copy(h_sb[:, q % 2, :, EV_D, :],
                                      h_ps[EV_D].rearrange("p (r n) -> p r n", r=R)).then_inc(s_hed, 1)

            def residue(m):
                dve.wait_ge(s_y, m + 1)
                dve.wait_ge(s_xte, m + 1)
                v = x1_flat[:, bass.ds(m * BANK, BANK)]
                nc.vector.tensor_tensor(v, y_ps, v, ALU.add).then_inc(s_x1, 1)

            def both(it, early):
                statistics(it, False)
                for q in range(GROUPS):
                    n = it * GROUPS + q
                    m = n - GROUPS
                    evacuate(m, q, early and q < 2)
                    masks(n, q, False)
                    residual(n, q, False)
                    if not (early and q == 0):
                        residue(m - 1)
                    low(n, q)

            statistics(0, True)
            for q in range(GROUPS):
                masks(q, q, True)
                residual(q, q, True)
                low(q, q)
            both(1, True)
            with dve.Fori(2, PAIRS) as it:
                both(it, False)
            for q in range(GROUPS):
                evacuate((PAIRS - 1) * GROUPS + q, q, False)
                residue((PAIRS - 1) * GROUPS + q - 1)
            residue(PAIRS * GROUPS - 1)

            def scaled(it, k):
                s = it * TILES + k
                dve.wait_ge(s_bc, s + 1)
                if not (at(it, 0) and k < 2):
                    dve.wait_ge(s_mm, s - 1)
                src = x1[:, k] if at(it, 0) else g[:, k]
                nc.vector.tensor_tensor(z[:, k % 2], rb_ps, src, ALU.mult).then_inc(s_z, 1)

            def slot(it, k, prev):
                e = (k - LAG_Z) % TILES
                if k >= LAG_Z:
                    if not at(it, STEPS + 1):
                        scaled(it, e)
                elif prev is not None:
                    scaled(prev, e)
                if at(it, STEPS + 1):
                    return
                s = it * TILES + k
                par = (k // 2) % 2
                dve.wait_ge(s_tr, s + 1)
                for b in range(TG):
                    last = nc.vector.bn_stats(st[:, par, (k % 2) * TG + b], gt_ps[k % 2][:, b * P:(b + 1) * P])
                last.then_inc(s_bn, 1)
                if k % 2 == 1:
                    dve.wait_ge(s_bn, s + 1)
                    root((ny[:, par], st[:, par]), (PAIRS + it * PAIRS + k // 2) * CHAIN)

            for k in range(TILES):
                slot(0, k, None)
            for k in range(TILES):
                slot(1, k, 0)
            with dve.Fori(2, STEPS + 1) as it:
                for k in range(TILES):
                    slot(it, k, it - 1)
            for k in range(LAG_Z):
                slot(STEPS + 1, k, STEPS)
            for k in range(TILES):
                dve.wait_ge(s_ev, STEPS * TILES + k + 1)
                if k >= 2:
                    dve.wait_ge(s_ot, k - 1)
                nc.vector.scalar_tensor_tensor(out=fin[:, k % 2], in0=H[:, k], scalar=1.0 / HSCALE,
                                               in1=x1[:, k], op0=ALU.mult, op1=ALU.add).then_inc(s_fin, 1)

        @block.tensor
        def _(pe):
            def transpose_group(n, q, first):
                pe.wait_ge(s_cast, n + 1)
                if not (first and q < 2):
                    pe.wait_ge(s_ate, n - 1)
                for j in range(GROUP):
                    last = nc.tensor.transpose(adj_ps[q % 2][:, j * P:(j + 1) * P],
                                               adj_b[:, q, j * P:(j + 1) * P], ident_b[:])
                last.then_inc(s_at, 1)
                if not (first and q == 0):
                    pe.wait_ge(s_xte, n)
                for j in range(GROUP):
                    last = nc.tensor.transpose(xt_ps[:, j * P:(j + 1) * P],
                                               x_in[:, q // 2, (q % 2) * GROUP + j], ident[:])
                last.then_inc(s_xt, 1)

            def gather(m, q, first):
                pe.wait_ge(s_mask, m + 1)
                pe.wait_ge(s_lo, m + 1)
                for j in range(GROUP):
                    if not (first and q == 0):
                        if j == EV_D:
                            pe.wait_ge(s_hed, m)
                        else:
                            pe.wait_ge(s_hea, (m - 1) * EV_D + j + 1)
                    for c in range(3):
                        last = nc.tensor.matmul(h_ps[j].rearrange("p (r n) -> p r n", r=R),
                                                part[:, q, c, j * P:(j + 1) * P],
                                                mask[:, q, :, j * P:(j + 1) * P],
                                                start=(c == 0), stop=(c == 2))
                    last.then_inc(s_h, 1)

            def weigh(m, q, first):
                pe.wait_ge(s_hea, (m + 1) * EV_D)
                pe.wait_ge(s_hed, m + 1)
                if not first:
                    pe.wait_ge(s_x1, m)
                for r in range(R):
                    last = nc.tensor.matmul(y_ps, gw_sb[:, r],
                                            h_sb[:, q % 2, r].rearrange("p a b -> p (a b)"),
                                            start=(r == 0), stop=(r == R - 1))
                last.then_inc(s_y, 1)

            def both(it, first):
                for q in range(GROUPS):
                    n = it * GROUPS + q
                    m = n - GROUPS
                    transpose_group(n, q, False)
                    gather(m, q, first)
                    if not (first and q == 0):
                        weigh(m - 1, (q - 1) % 2, first and q == 1)

            pe.wait_ge(s_id, 1)
            pe.wait_ge(s_x[0], 16)
            for q in range(GROUPS):
                if q == 2:
                    pe.wait_ge(s_x[1], 16)
                transpose_group(q, q, True)
            pe.wait_ge(s_wc, 1)
            nc.tensor.transpose(y_ps[:, 0:P], wcent[:], ident[:]).then_inc(s_wt, 1)
            pe.wait_ge(s_we, 1)
            both(1, True)
            with pe.Fori(2, PAIRS) as it:
                both(it, False)
            last_m = (PAIRS - 1) * GROUPS
            for q in range(GROUPS):
                gather(last_m + q, q, False)
                weigh(last_m + q - 1, (q - 1) % 2, False)
            weigh(last_m + GROUPS - 1, (GROUPS - 1) % 2, False)

            def turn(it, k):
                s = it * TILES + k
                if not at(it, 0):
                    pe.wait_ge(s_silu, s + 1 - TILES)
                if not (at(it, 0) and k < 2):
                    pe.wait_ge(s_bn, s - 1)
                src = x1[:, k] if at(it, 0) else g[:, k]
                for b in range(TG):
                    last = nc.tensor.transpose(gt_ps[k % 2][:, b * P:(b + 1) * P],
                                               src[:, b * P:(b + 1) * P], ident[:])
                last.then_inc(s_tr, 1)

            def broadcast(it, k):
                s = it * TILES + k
                if k % 2 == 0:
                    pe.wait_ge(s_chain, (PAIRS + it * PAIRS + k // 2 + 1) * CHAIN)
                if not (at(it, 0) and k == 0):
                    pe.wait_ge(s_z, s)
                par = (k // 2) % 2
                for b in range(TG):
                    c = (k % 2) * TG + b
                    last = nc.tensor.transpose(rb_ps[:, b * P:(b + 1) * P],
                                               ny[:, par, c:c + 1].to_broadcast([P, P]), ident[:])
                last.then_inc(s_bc, 1)

            def linear(it, k):
                s = it * TILES + k
                pe.wait_ge(s_z, s + 1)
                if not (at(it, 0) and k == 0):
                    pe.wait_ge(s_ev, s)
                m = cent if at(it, 0) else weff
                for a in range(TILE // BANK):
                    last = nc.tensor.matmul(mm_ps[:, a * BANK:(a + 1) * BANK], m[:],
                                            z[:, k % 2, a * BANK:(a + 1) * BANK], start=True, stop=True)
                last.then_inc(s_mm, 1)

            def slot(it, k, prev):
                if k >= LAG_Z:
                    if not at(it, STEPS + 1):
                        broadcast(it, k - LAG_Z)
                elif prev is not None:
                    broadcast(prev, (k - LAG_Z) % TILES)
                if not at(it, STEPS + 1):
                    turn(it, k)
                if k >= LAG_MM:
                    if not at(it, STEPS + 1):
                        linear(it, k - LAG_MM)
                elif prev is not None:
                    linear(prev, (k - LAG_MM) % TILES)

            pe.wait_ge(s_x1, PAIRS * GROUPS)
            for k in range(TILES):
                slot(0, k, None)
            for k in range(TILES):
                slot(1, k, 0)
            with pe.Fori(2, STEPS + 1) as it:
                for k in range(TILES):
                    slot(it, k, it - 1)
            for k in range(LAG_MM):
                slot(STEPS + 1, k, STEPS)
            for k in range(TILES):
                pe.wait_ge(s_fin, k + 1)
                if k >= 2:
                    pe.wait_ge(s_oe, k - 1)
                else:
                    pe.wait_ge(s_bn, (STEPS + 1) * TILES)
                for b in range(TG):
                    last = nc.tensor.transpose(gt_ps[k % 2][:, b * P:(b + 1) * P],
                                               fin[:, k % 2, b * P:(b + 1) * P], ident[:])
                last.then_inc(s_ot, 1)


_INS = ["x", "adj", "L0_gnn_weight", "L0_gnn_bias", "L0_ffn_ln_w", "L0_ffn_ln_b", "L0_ffn_W", "L0_ffn_b"]


def kernel(**inputs):
    import numpy as _np
    import concourse.bacc as _bacc
    from concourse import mybir as _mybir
    from concourse.bass_utils import run_bass_kernel_spmd as _run

    nc = _bacc.Bacc("TRN2", target_bir_lowering=False, num_devices=1)
    arrays, args = {}, []
    for name in _INS:
        a = _np.ascontiguousarray(inputs[name])
        arrays[f"in_{name}"] = a
        args.append(nc.dram_tensor(f"in_{name}", a.shape, _mybir.dt.from_np(a.dtype), kind="ExternalInput").ap())
    args.append(nc.dram_tensor("out_0", inputs["x"].shape, _mybir.dt.float32, kind="ExternalOutput").ap())
    build(nc, *args)
    r = _run(nc, [arrays], core_ids=[0])
    return r.results[0]["out_0"]
```

```python
import math
from contextlib import ExitStack

import concourse.bass as bass
from concourse import mybir

FP32 = mybir.dt.float32
BF16 = mybir.dt.bfloat16
I32 = mybir.dt.int32
ALU = mybir.AluOpType
ACT = mybir.ActivationFunctionType
AX = mybir.AxisListType

P = 128
B = 64
R = 4
STEPS = 30
EPS = 1e-5
BANK = 512

GROUP = BANK // P
TG = 8
TILE = TG * P
TILES = B // TG
PAIR = 2 * TG
GROUPS = PAIR // GROUP
PAIRS = B // PAIR

ROOT = math.sqrt(P)
MAGIC = 1597463007.0
NEWTON = 3
CHAIN = 5 + 3 * NEWTON
TAU = 0.01
HSCALE = 1 / TAU

SPLIT = ((), (0,), (1, 2), (3,))

LAG_Z, LAG_MM, LAG_EV = 4, 5, 7


def at(it, n):
    return isinstance(it, int) and it == n


def build(nc, x, adj, gw, gb, ln_w, ln_b, fw, fb, out):
    ctx = ExitStack()
    with ctx:
        def sb(name, shape, dt=FP32):
            return ctx.enter_context(nc.sbuf_tensor(name, shape, dt))

        def sem(name):
            return ctx.enter_context(nc.semaphore(name))

        x_v = x.rearrange("b n c -> n b c")
        adj_v = adj.rearrange("b n m -> n b m")
        out_v = out.rearrange("b n c -> n b c")

        ident = sb("ident", [P, P])
        ident_b = sb("ident_b", [P, P], BF16)
        gw_sb = sb("gw_sb", [P, R, P])
        gb_sb = sb("gb_sb", [P, 1])
        fw_sb = sb("fw_sb", [P, P])
        fb_sb = sb("fb_sb", [P, 1])
        lnw_row = sb("lnw_row", [P, P])
        lnb_row = sb("lnb_row", [P, P])
        fww = sb("fww", [P, P])
        fwb = sb("fwb", [P, P])
        wsum = sb("wsum", [P, 1])
        bsum = sb("bsum", [P, 1])
        wcent = sb("wcent", [P, P])
        weff = sb("weff", [P, P])
        cent = sb("cent", [P, P])
        bias100 = sb("bias100", [P, 1])
        zero = sb("zero", [P, 1])

        x_in = sb("x_in", [P, 2, TG, P])
        adj_in = sb("adj_in", [P, 2, TG, P], I32)
        adj_b = sb("adj_b", [P, GROUPS, BANK], BF16)
        adj_t = sb("adj_t", [P, GROUPS, BANK], BF16)
        mask = sb("mask", [P, GROUPS, R, BANK], BF16)
        xn = sb("xn", [P, GROUPS, BANK])
        xres = sb("xres", [P, GROUPS, BANK])
        part = sb("part", [P, GROUPS, 3, BANK], BF16)
        h_sb = sb("h_sb", [P, 2, R, GROUP, P])
        rstd = sb("rstd", [P, PAIR])
        nmr = sb("nmr", [P, PAIR])
        msum = sb("msum", [P, PAIR])

        x1_flat = sb("x1", [P, B * P])
        x1 = x1_flat[:].rearrange("p (k t) -> p k t", k=TILES)
        H = sb("H", [P, TILES, TILE])
        T = sb("T", [P, 2, TILE])
        U = sb("U", [P, 2, TILE])
        g = H
        z = sb("z", [P, 2, TILE])
        fin = sb("fin", [P, 2, TILE])
        o_sb = sb("o_sb", [P, 2, TILE])
        st = sb("st", [P, 2, PAIR, 6])
        nv = sb("nv", [P, PAIR])
        nd = sb("nd", [P, PAIR])
        nt = sb("nt", [P, PAIR])
        ny = sb("ny", [P, 2, PAIR])

        ps = ctx.enter_context(nc.psum_tensor("ps", [P, 8, BANK], FP32))
        adj_ps = [ps[:, b, 0:BANK // 2].bitcast(BF16) for b in (0, 1)]
        h_ps = [ps[:, 2 + j, :] for j in range(GROUP)]
        xt_ps = ps[:, 6, :]
        y_ps = ps[:, 7, :]
        gt_ps = [ps[:, 0:2, :].rearrange("p a b -> p (a b)"), ps[:, 2:4, :].rearrange("p a b -> p (a b)")]
        rb_ps = ps[:, 4:6, :].rearrange("p a b -> p (a b)")
        mm_ps = ps[:, 6:8, :].rearrange("p a b -> p (a b)")

        s_w = sem("s_w")
        s_x = [sem("s_xin0"), sem("s_xin1")]
        s_adj = [sem("s_adj0"), sem("s_adj1")]
        s_id0 = sem("s_id0")
        s_id = sem("s_id")
        s_prep = sem("s_prep")
        s_wc = sem("s_wc")
        s_wt = sem("s_wt")
        s_we = sem("s_we")
        s_xbn = sem("s_xbn")
        s_chain = sem("s_chain")
        s_m = sem("s_m")
        s_ln = sem("s_ln")
        s_cast = sem("s_cast")
        s_xs = sem("s_xs")
        s_xn = sem("s_xn")
        s_hi = sem("s_hi")
        s_res = sem("s_res")
        s_mid = sem("s_mid")
        s_lo = sem("s_lo")
        s_at = sem("s_at")
        s_ate = sem("s_ate")
        s_xt = sem("s_xt")
        s_xte = sem("s_xte")
        s_mask = sem("s_mask")
        s_h = sem("s_h")
        s_he = sem("s_he")
        s_y = sem("s_y")
        s_x1 = sem("s_x1")
        s_tanh = sem("s_tanh")
        s_add = sem("s_add")
        s_silu = sem("s_silu")
        s_tr = sem("s_tr")
        s_bn = sem("s_bn")
        s_bc = sem("s_bc")
        s_z = sem("s_z")
        s_mm = sem("s_mm")
        s_ev = sem("s_ev")
        s_fin = sem("s_fin")
        s_ot = sem("s_ot")
        s_oe = sem("s_oe")
        s_out = [sem("s_out0"), sem("s_out1")]

        block = ctx.enter_context(nc.Block())
        N_W = 6

        @block.sync
        def _(sp):
            def load_pair(it, first):
                for t in range(2):
                    if not first:
                        sp.wait_ge(s_xn, it * GROUPS + 2 * t + 2 - GROUPS)
                        sp.wait_ge(s_xt, it * GROUPS + 2 * t + 2 - GROUPS)
                    sp.dma_start(x_in[:, t], x_v[:, bass.ds(it * PAIR + t * TG, TG), :]).then_inc(s_x[t], 16)
                    if not first:
                        sp.wait_ge(s_cast, it * GROUPS + 2 * t + 2 - GROUPS)
                    sp.dma_start(adj_in[:, t], adj_v[:, bass.ds(it * PAIR + t * TG, TG), :]).then_inc(s_adj[t], 16)

            load_pair(0, True)
            with sp.Fori(1, PAIRS) as it:
                load_pair(it, False)
            for k in range(TILES):
                sp.wait_ge(s_oe, k + 1)
                sp.dma_start(out_v[:, k * TG:(k + 1) * TG, :],
                             o_sb[:, k % 2].rearrange("p (b c) -> p b c", c=P)).then_inc(s_out[k % 2], 16)
            for a in range(2):
                sp.wait_ge(s_out[a], 16 * TILES // 2)

        @block.gpsimd
        def _(pool):
            nc.gpsimd.memset(ident[:], 0.0)
            nc.gpsimd.memset(ident_b[:], 0.0).then_inc(s_id0, 1)
            pool.wait_ge(s_id0, 1)
            for m in (ident, ident_b):
                last = nc.gpsimd.affine_select(out=m[:], in_=m[:], compare_op=ALU.not_equal, fill=1.0,
                                               base=0, pattern=[[-1, P]], channel_multiplier=1)
            last.then_inc(s_id, 1)

            def prepare(it, first):
                for q in range(GROUPS):
                    t, o = q // 2, (q % 2) * GROUP
                    n = it * GROUPS + q
                    b = slice(q * GROUP, (q + 1) * GROUP)
                    dst = xn[:, q].rearrange("p (b c) -> p b c", c=P)
                    if q == 0:
                        pool.wait_ge(s_ln, it + 1)
                    if not first:
                        pool.wait_ge(s_res, n + 1 - GROUPS)
                    nc.gpsimd.tensor_tensor(dst, x_in[:, t, o:o + GROUP, :],
                                            rstd[:, b].unsqueeze(2).to_broadcast([P, GROUP, P]),
                                            ALU.mult).then_inc(s_xs, 1)
                    pool.wait_ge(s_xs, n + 1)
                    nc.gpsimd.tensor_tensor(dst, dst, nmr[:, b].unsqueeze(2).to_broadcast([P, GROUP, P]),
                                            ALU.add).then_inc(s_xn, 1)

            prepare(0, True)
            with pool.Fori(1, PAIRS) as it:
                prepare(it, False)

            def add(it, k, early):
                pool.wait_ge(s_tanh, (it - 1) * TILES + k + 1)
                if not (early and k < 2):
                    pool.wait_ge(s_silu, (it - 1) * TILES + k - 1)
                nc.gpsimd.tensor_tensor(U[:, k % 2], H[:, k], T[:, k % 2], ALU.add).then_inc(s_add, 1)

            for k in range(TILES):
                add(1, k, True)
            with pool.Fori(2, STEPS + 1) as it:
                for k in range(TILES):
                    add(it, k, False)

        @block.scalar
        def _(act):
            act.dma_start(gw_sb[:], gw.rearrange("r d o -> d r o")).then_inc(s_w, 16)
            act.dma_start(gb_sb[:], gb.rearrange("(o a) -> o a", a=1)).then_inc(s_w, 16)
            act.dma_start(fw_sb[:], fw).then_inc(s_w, 16)
            act.dma_start(fb_sb[:], fb.rearrange("(o a) -> o a", a=1)).then_inc(s_w, 16)
            act.dma_start(lnw_row[:], ln_w.rearrange("(a c) -> a c", a=1).to_broadcast([P, P])).then_inc(s_w, 16)
            act.dma_start(lnb_row[:], ln_b.rearrange("(a c) -> a c", a=1).to_broadcast([P, P])).then_inc(s_w, 16)

            def cast(n, q, it, first):
                act.wait_ge(s_adj[q // 2], it * 16 + 16)
                if not first:
                    act.wait_ge(s_at, n + 1 - GROUPS)
                o = (q % 2) * GROUP
                nc.scalar.copy(adj_b[:, q].rearrange("p (b m) -> p b m", m=P),
                               adj_in[:, q // 2, o:o + GROUP, :]).then_inc(s_cast, 1)

            def prepare_a(n, q, first):
                act.wait_ge(s_at, n + 1)
                if not first:
                    act.wait_ge(s_mask, n + 1 - GROUPS)
                nc.scalar.copy(adj_t[:, q], adj_ps[q % 2]).then_inc(s_ate, 1)
                if at(n, 0):
                    act.wait_ge(s_w, 16 * N_W)
                act.wait_ge(s_xt, n + 1)
                nc.scalar.activation(x1_flat[:, bass.ds(n * BANK, BANK)], xt_ps, ACT.Identity,
                                     bias=gb_sb[:, 0:1]).then_inc(s_xte, 1)

            def prepare_b(n, q, first):
                act.wait_ge(s_xn, n + 1)
                if not first:
                    act.wait_ge(s_h, (n + 1 - GROUPS) * GROUP)
                nc.scalar.copy(part[:, q, 0], xn[:, q]).then_inc(s_hi, 1)
                act.wait_ge(s_res, n + 1)
                nc.scalar.copy(part[:, q, 1], xres[:, q]).then_inc(s_mid, 1)

            def evacuate(m, q, early):
                if not early:
                    act.wait_ge(s_y, m - 1)
                for j in range(GROUP):
                    act.wait_ge(s_h, m * GROUP + j + 1)
                    nc.scalar.copy(h_sb[:, q % 2, :, j, :],
                                   h_ps[j].rearrange("p (r n) -> p r n", r=R)).then_inc(s_he, 1)

            def both(it, early):
                cast(it * GROUPS, 0, it, False)
                for q in range(GROUPS):
                    n = it * GROUPS + q
                    if q + 1 < GROUPS:
                        cast(n + 1, q + 1, it, False)
                    evacuate(n - GROUPS, q, early and q < 2)
                    prepare_a(n, q, False)
                    for p in SPLIT[q]:
                        prepare_b(it * GROUPS + p, p, False)

            for q in range(GROUPS):
                cast(q, q, 0, True)
            for q in range(GROUPS):
                prepare_a(q, q, True)
                prepare_b(q, q, True)
            both(1, True)
            with act.Fori(2, PAIRS) as it:
                both(it, False)
            for q in range(GROUPS):
                evacuate((PAIRS - 1) * GROUPS + q, q, False)

            def tanh(it, k, early):
                act.wait_ge(s_ev, it * TILES + k + 1 - TILES)
                if not early:
                    act.wait_ge(s_add, (it - 1) * TILES + k - 1)
                nc.scalar.activation(T[:, k % 2], H[:, k], ACT.Tanh, scale=1.0 / HSCALE).then_inc(s_tanh, 1)

            def silu(it, k):
                act.wait_ge(s_add, (it - 1) * TILES + k + 1)
                nc.scalar.activation(g[:, k], U[:, k % 2], ACT.Silu, scale=1.0 / HSCALE).then_inc(s_silu, 1)

            def evac(it, k):
                act.wait_ge(s_mm, it * TILES + k + 1)
                bias = zero if at(it, 0) else bias100
                nc.scalar.activation(H[:, k], mm_ps, ACT.Identity, bias=bias[:, 0:1],
                                     scale=HSCALE).then_inc(s_ev, 1)

            def slot(it, k, prev):
                if not at(it, 0) and not at(it, STEPS + 1):
                    tanh(it, k, at(it, 1) and k < 2)
                if k >= 1:
                    if not at(it, 0) and not at(it, STEPS + 1):
                        silu(it, k - 1)
                elif prev is not None and not at(prev, 0):
                    silu(prev, TILES - 1)
                e = (k - LAG_EV) % TILES
                if k >= LAG_EV:
                    evac(it, e)
                elif prev is not None:
                    evac(prev, e)

            act.wait_ge(s_wt, 1)
            nc.scalar.copy(weff[:], mm_ps[:, 0:P]).then_inc(s_we, 1)
            for k in range(TILES):
                slot(0, k, None)
            for k in range(TILES):
                slot(1, k, 0)
            with act.Fori(2, STEPS + 1) as it:
                for k in range(TILES):
                    slot(it, k, it - 1)
            for k in range(LAG_EV):
                slot(STEPS + 1, k, STEPS)
            for k in range(TILES):
                act.wait_ge(s_ot, k + 1)
                if k >= 2:
                    act.wait_ge(s_out[k % 2], 16 * (k // 2))
                nc.scalar.copy(o_sb[:, k % 2], gt_ps[k % 2]).then_inc(s_oe, 1)

        @block.vector
        def _(dve):
            def step(ins, semaphore, value):
                ins.then_inc(semaphore, 1)
                dve.wait_ge(semaphore, value)

            def root(n, y, stats, base):
                if n > 1:
                    dve.wait_ge(s_chain, base + n - 1)
                even, odd = stats[:, :, 1:3], stats[:, :, 4:6]
                if n == 1:
                    ins = nc.vector.tensor_tensor(nd[:], even[:, :, 0], odd[:, :, 0], ALU.subtract)
                elif n == 2:
                    ins = nc.vector.scalar_tensor_tensor(out=nt[:], in0=nd[:], scalar=P / 4.0, in1=nd[:],
                                                         op0=ALU.mult, op1=ALU.mult)
                elif n == 3:
                    ins = nc.vector.scalar_tensor_tensor(out=nd[:], in0=nt[:], scalar=P * EPS,
                                                         in1=even[:, :, 1], op0=ALU.add, op1=ALU.add)
                elif n == 4:
                    ins = nc.vector.tensor_tensor(nv[:], nd[:], odd[:, :, 1], ALU.add)
                elif n == 5:
                    ins = nc.vector.tensor_scalar(y.bitcast(I32), nv[:].bitcast(I32), -0.5, MAGIC,
                                                  ALU.mult, ALU.add)
                elif n % 3 == 0:
                    ins = nc.vector.tensor_tensor(nt[:], y, y, ALU.mult)
                elif n % 3 == 1:
                    ins = nc.vector.scalar_tensor_tensor(out=nd[:], in0=nt[:], scalar=-0.5, in1=nv[:],
                                                         op0=ALU.mult, op1=ALU.mult)
                else:
                    ins = nc.vector.scalar_tensor_tensor(out=y, in0=nd[:], scalar=1.5, in1=y,
                                                         op0=ALU.add, op1=ALU.mult)
                ins.then_inc(s_chain, 1)

            def statistics(it, first):
                for b in range(PAIR):
                    if b % TG == 0:
                        dve.wait_ge(s_x[b // TG], it * 16 + 16)
                    last = nc.vector.bn_stats(st[:, 0, b], x_in[:, b // TG, b % TG])
                last.then_inc(s_xbn, 1)
                dve.wait_ge(s_xbn, it + 1)
                for i in range(1, CHAIN + 1):
                    root(i, ny[:, 0], st[:, 0], it * CHAIN)
                dve.wait_ge(s_chain, (it + 1) * CHAIN)
                step(nc.vector.tensor_tensor(msum[:], st[:, 0, :, 1], st[:, 0, :, 4], ALU.add), s_m, it * 2 + 1)
                if not first:
                    dve.wait_ge(s_xn, it * GROUPS)
                step(nc.vector.tensor_scalar(rstd[:], ny[:, 0], ROOT, None, ALU.mult), s_m, it * 2 + 2)
                nc.vector.scalar_tensor_tensor(out=nmr[:], in0=msum[:], scalar=-0.5, in1=rstd[:],
                                               op0=ALU.mult, op1=ALU.mult).then_inc(s_ln, 1)

            def residual(n, q, first):
                dve.wait_ge(s_hi, n + 1)
                if not first:
                    dve.wait_ge(s_mid, n + 1 - GROUPS)
                nc.vector.tensor_tensor(xres[:, q], xn[:, q], part[:, q, 0], ALU.subtract).then_inc(s_res, 1)

            def low(n, q):
                dve.wait_ge(s_mid, n + 1)
                nc.vector.tensor_tensor(part[:, q, 2], xres[:, q], part[:, q, 1], ALU.subtract).then_inc(s_lo, 1)

            def masks(n, q, first):
                dve.wait_ge(s_ate, n + 1)
                if not first:
                    dve.wait_ge(s_h, (n + 1 - GROUPS) * GROUP)
                for r in range(R):
                    last = nc.vector.tensor_scalar(mask[:, q, r], adj_t[:, q], float(r + 1), None, ALU.is_equal)
                last.then_inc(s_mask, 1)

            def residue(m):
                dve.wait_ge(s_y, m + 1)
                dve.wait_ge(s_xte, m + 1)
                v = x1_flat[:, bass.ds(m * BANK, BANK)]
                nc.vector.tensor_tensor(v, y_ps, v, ALU.add).then_inc(s_x1, 1)

            def both(it, early):
                for q in range(GROUPS):
                    n = it * GROUPS + q
                    m = n - GROUPS
                    if q == 0:
                        statistics(it, False)
                    masks(n, q, False)
                    if not (early and q == 0):
                        residue(m - 1)
                    for p in SPLIT[q]:
                        residual(it * GROUPS + p, p, False)
                        low(it * GROUPS + p, p)

            nc.vector.memset(zero[:], 0.0)
            statistics(0, True)

            dve.wait_ge(s_w, 16 * N_W)
            dve.wait_ge(s_id, 1)
            nc.vector.tensor_tensor(fww[:], fw_sb[:], lnw_row[:], ALU.mult)
            step(nc.vector.tensor_tensor(fwb[:], fw_sb[:], lnb_row[:], ALU.mult), s_prep, 1)
            nc.vector.reduce_sum(wsum[:], fww[:], AX.X)
            step(nc.vector.reduce_sum(bsum[:], fwb[:], AX.X), s_prep, 2)
            step(nc.vector.tensor_scalar(wsum[:], wsum[:], 1.0 / P, None, ALU.mult), s_prep, 3)
            nc.vector.tensor_scalar(wcent[:], fww[:], wsum[:, 0:1], ROOT, ALU.subtract, ALU.mult)
            nc.vector.tensor_scalar(cent[:], ident[:], 1.0 / P, ROOT, ALU.subtract, ALU.mult)
            nc.vector.tensor_scalar(bias100[:], bsum[:], fb_sb[:, 0:1], HSCALE, ALU.add,
                                    ALU.mult).then_inc(s_wc, 1)

            for q in range(GROUPS):
                masks(q, q, True)
                residual(q, q, True)
                low(q, q)
            both(1, True)
            with dve.Fori(2, PAIRS) as it:
                both(it, False)
            for q in range(GROUPS):
                residue((PAIRS - 1) * GROUPS + q - 1)
            residue(PAIRS * GROUPS - 1)

            def scaled(it, k):
                s = it * TILES + k
                dve.wait_ge(s_bc, s + 1)
                if not (at(it, 0) and k < 2):
                    dve.wait_ge(s_mm, s - 1)
                src = x1[:, k] if at(it, 0) else g[:, k]
                nc.vector.tensor_tensor(z[:, k % 2], rb_ps, src, ALU.mult).then_inc(s_z, 1)

            def slot(it, k, prev):
                pair = it if k >= 2 else prev
                if at(pair, STEPS + 1):
                    pair = None
                c = ((k - 2) // 2) % PAIRS
                early = k % 2 == 0

                def fill(n):
                    if pair is not None and n <= CHAIN:
                        root(n, ny[:, c % 2], st[:, c % 2], (PAIRS + pair * PAIRS + c) * CHAIN)

                e = (k - LAG_Z) % TILES
                if k >= LAG_Z:
                    if not at(it, STEPS + 1):
                        scaled(it, e)
                elif prev is not None:
                    scaled(prev, e)
                if early and pair is not None:
                    dve.wait_ge(s_bn, pair * TILES + 2 * c + 2)
                for n in (1, 2) if early else (TG + 3, TG + 4):
                    fill(n)
                if not at(it, STEPS + 1):
                    dve.wait_ge(s_tr, it * TILES + k + 1)
                for b in range(TG):
                    if not at(it, STEPS + 1):
                        last = nc.vector.bn_stats(st[:, (k // 2) % 2, (k % 2) * TG + b],
                                                  gt_ps[k % 2][:, b * P:(b + 1) * P])
                        if b == TG - 1:
                            last.then_inc(s_bn, 1)
                    fill((3 if early else TG + 5) + b)

            for k in range(TILES):
                slot(0, k, None)
            for k in range(TILES):
                slot(1, k, 0)
            with dve.Fori(2, STEPS + 1) as it:
                for k in range(TILES):
                    slot(it, k, it - 1)
            for k in range(LAG_Z):
                slot(STEPS + 1, k, STEPS)
            for k in range(TILES):
                dve.wait_ge(s_ev, STEPS * TILES + k + 1)
                if k >= 2:
                    dve.wait_ge(s_ot, k - 1)
                nc.vector.scalar_tensor_tensor(out=fin[:, k % 2], in0=H[:, k], scalar=1.0 / HSCALE,
                                               in1=x1[:, k], op0=ALU.mult, op1=ALU.add).then_inc(s_fin, 1)

        @block.tensor
        def _(pe):
            def transpose_group(n, q, first):
                pe.wait_ge(s_cast, n + 1)
                if not (first and q < 2):
                    pe.wait_ge(s_ate, n - 1)
                for j in range(GROUP):
                    last = nc.tensor.transpose(adj_ps[q % 2][:, j * P:(j + 1) * P],
                                               adj_b[:, q, j * P:(j + 1) * P], ident_b[:])
                last.then_inc(s_at, 1)
                if not (first and q == 0):
                    pe.wait_ge(s_xte, n)
                for j in range(GROUP):
                    last = nc.tensor.transpose(xt_ps[:, j * P:(j + 1) * P],
                                               x_in[:, q // 2, (q % 2) * GROUP + j], ident[:])
                last.then_inc(s_xt, 1)

            def gather(m, q, first):
                pe.wait_ge(s_mask, m + 1)
                pe.wait_ge(s_lo, m + 1)
                for j in range(GROUP):
                    if not (first and q == 0):
                        pe.wait_ge(s_he, (m - 1) * GROUP + j + 1)
                    for c in range(3):
                        last = nc.tensor.matmul(h_ps[j].rearrange("p (r n) -> p r n", r=R),
                                                part[:, q, c, j * P:(j + 1) * P],
                                                mask[:, q, :, j * P:(j + 1) * P],
                                                start=(c == 0), stop=(c == 2))
                    last.then_inc(s_h, 1)

            def weigh(m, q, first):
                pe.wait_ge(s_he, (m + 1) * GROUP)
                if not first:
                    pe.wait_ge(s_x1, m)
                for r in range(R):
                    last = nc.tensor.matmul(y_ps, gw_sb[:, r],
                                            h_sb[:, q % 2, r].rearrange("p a b -> p (a b)"),
                                            start=(r == 0), stop=(r == R - 1))
                last.then_inc(s_y, 1)

            def both(it, first):
                for q in range(GROUPS):
                    n = it * GROUPS + q
                    m = n - GROUPS
                    gather(m, q, first)
                    transpose_group(n, q, False)
                    if not (first and q == 0):
                        weigh(m - 1, (q - 1) % 2, first and q == 1)

            pe.wait_ge(s_id, 1)
            pe.wait_ge(s_x[0], 16)
            for q in range(GROUPS):
                if q == 2:
                    pe.wait_ge(s_x[1], 16)
                transpose_group(q, q, True)
            pe.wait_ge(s_w, 16 * N_W)
            both(1, True)
            with pe.Fori(2, PAIRS) as it:
                both(it, False)
            last_m = (PAIRS - 1) * GROUPS
            for q in range(GROUPS):
                gather(last_m + q, q, False)
                weigh(last_m + q - 1, (q - 1) % 2, False)
            weigh(last_m + GROUPS - 1, (GROUPS - 1) % 2, False)

            def turn(it, k):
                s = it * TILES + k
                if not at(it, 0):
                    pe.wait_ge(s_silu, s + 1 - TILES)
                if not (at(it, 0) and k < 2):
                    pe.wait_ge(s_bn, s - 1)
                src = x1[:, k] if at(it, 0) else g[:, k]
                for b in range(TG):
                    last = nc.tensor.transpose(gt_ps[k % 2][:, b * P:(b + 1) * P],
                                               src[:, b * P:(b + 1) * P], ident[:])
                last.then_inc(s_tr, 1)

            def broadcast(it, k):
                s = it * TILES + k
                if k % 2 == 0:
                    pe.wait_ge(s_chain, (PAIRS + it * PAIRS + k // 2 + 1) * CHAIN)
                if not (at(it, 0) and k == 0):
                    pe.wait_ge(s_z, s)
                par = (k // 2) % 2
                for b in range(TG):
                    c = (k % 2) * TG + b
                    last = nc.tensor.transpose(rb_ps[:, b * P:(b + 1) * P],
                                               ny[:, par, c:c + 1].to_broadcast([P, P]), ident[:])
                last.then_inc(s_bc, 1)

            def linear(it, k):
                s = it * TILES + k
                pe.wait_ge(s_z, s + 1)
                if at(it, 0) and k == 0:
                    pe.wait_ge(s_we, 1)
                else:
                    pe.wait_ge(s_ev, s)
                m = cent if at(it, 0) else weff
                for a in range(TILE // BANK):
                    last = nc.tensor.matmul(mm_ps[:, a * BANK:(a + 1) * BANK], m[:],
                                            z[:, k % 2, a * BANK:(a + 1) * BANK], start=True, stop=True)
                last.then_inc(s_mm, 1)

            def slot(it, k, prev):
                if k >= LAG_Z:
                    if not at(it, STEPS + 1):
                        broadcast(it, k - LAG_Z)
                elif prev is not None:
                    broadcast(prev, (k - LAG_Z) % TILES)
                if not at(it, STEPS + 1):
                    turn(it, k)
                if k >= LAG_MM:
                    if not at(it, STEPS + 1):
                        linear(it, k - LAG_MM)
                elif prev is not None:
                    linear(prev, (k - LAG_MM) % TILES)

            pe.wait_ge(s_x1, PAIRS * GROUPS)
            pe.wait_ge(s_wc, 1)
            nc.tensor.transpose(mm_ps[:, 0:P], wcent[:], ident[:]).then_inc(s_wt, 1)
            for k in range(TILES):
                slot(0, k, None)
            for k in range(TILES):
                slot(1, k, 0)
            with pe.Fori(2, STEPS + 1) as it:
                for k in range(TILES):
                    slot(it, k, it - 1)
            for k in range(LAG_MM):
                slot(STEPS + 1, k, STEPS)
            for k in range(TILES):
                pe.wait_ge(s_fin, k + 1)
                if k >= 2:
                    pe.wait_ge(s_oe, k - 1)
                else:
                    pe.wait_ge(s_bn, (STEPS + 1) * TILES)
                for b in range(TG):
                    last = nc.tensor.transpose(gt_ps[k % 2][:, b * P:(b + 1) * P],
                                               fin[:, k % 2, b * P:(b + 1) * P], ident[:])
                last.then_inc(s_ot, 1)


_INS = ["x", "adj", "L0_gnn_weight", "L0_gnn_bias", "L0_ffn_ln_w", "L0_ffn_ln_b", "L0_ffn_W", "L0_ffn_b"]


def kernel(**inputs):
    import numpy as _np
    import concourse.bacc as _bacc
    from concourse import mybir as _mybir
    from concourse.bass_utils import run_bass_kernel_spmd as _run

    nc = _bacc.Bacc("TRN2", target_bir_lowering=False, num_devices=1)
    arrays, args = {}, []
    for name in _INS:
        a = _np.ascontiguousarray(inputs[name])
        arrays[f"in_{name}"] = a
        args.append(nc.dram_tensor(f"in_{name}", a.shape, _mybir.dt.from_np(a.dtype), kind="ExternalInput").ap())
    args.append(nc.dram_tensor("out_0", inputs["x"].shape, _mybir.dt.float32, kind="ExternalOutput").ap())
    build(nc, *args)
    r = _run(nc, [arrays], core_ids=[0])
    return r.results[0]["out_0"]
```
